# Optimizing a Trainium2 kernel written in Bass

```python
import numpy as np
import jax
import jax.numpy as jnp

def _softmax(x, axis=-1):
    return jax.nn.softmax(x, axis=axis)

def _gelu(x):
    return jax.nn.gelu(x, approximate=True)

def _silu(x):
    return jax.nn.silu(x)

def _sigmoid(x):
    return jax.nn.sigmoid(x)

def _layernorm(x, axis=-1, eps=1e-05):
    m = jnp.mean(x, axis=axis, keepdims=True)
    v = jnp.var(x, axis=axis, keepdims=True)
    return (x - m) / jnp.sqrt(v + eps)

def _scatter_add(tgt, idx, src, axis=0):
    return tgt.at[idx].add(src)

def _segment_sum(src, seg, n):
    return jax.ops.segment_sum(src, seg, n)
kernel_name = 'mk_cond_resid_d1_seqx_r4_3925ba'

def setup_inputs(seed: int=0):
    np.random.seed(seed)
    _w = jnp.asarray

    def _rec_inputs():
        import jax
        import jax.numpy as jnp
        _rk = jax.random.key(seed)
        x = -0.000125 + 0.9999 * jax.random.normal(jax.random.fold_in(_rk, 1), (64, 64, 256), jnp.float32)
        _lenS = 64 - jax.random.randint(jax.random.fold_in(_rk, 7), (64,), 0, max(1, 64 // 4) + 1, jnp.int32)
        _lenS2 = 64 - jax.random.randint(jax.random.fold_in(_rk, 8), (64,), 0, max(1, 64 // 4) + 1, jnp.int32)
        cond_512 = 0.0061147 + 1.02565 * jax.random.normal(jax.random.fold_in(_rk, 11), (64, 128), jnp.float32)
        return (x, cond_512)
    x, cond_512 = _rec_inputs()

    def _L0_cond_setup():
        import jax, jax.numpy as jnp
        import numpy as np
        B, S, D, H, C = (8, 1024, 256, 64, 128)
        INIT_RANGE = 0.01
        key = jax.random.key(seed)
        ks = jax.random.split(key, 6)
        return {'hidden_states': jax.random.normal(ks[0], (B, S, D), dtype=jnp.float32), 'conditions': jax.random.normal(ks[1], (B, C), dtype=jnp.float32), 'down_project': jax.random.normal(ks[2], (D, H), dtype=jnp.float32) * INIT_RANGE, 'down_gamma': jax.random.normal(ks[3], (C, H), dtype=jnp.float32), 'down_beta': jnp.zeros((C, H), dtype=jnp.float32), 'up_project': jax.random.normal(ks[4], (H, D), dtype=jnp.float32) * INIT_RANGE, 'up_gamma': jax.random.normal(ks[5], (C, D), dtype=jnp.float32), 'up_beta': jnp.zeros((C, D), dtype=jnp.float32)}
    _L0_cond_all = _L0_cond_setup()
    _L0_cond_in = {k: v for k, v in _L0_cond_all.items() if k in ('down_project', 'down_gamma', 'down_beta', 'up_project', 'up_gamma', 'up_beta')}
    del _L0_cond_all
    return {'x': x, 'cond_512': cond_512, 'L0_cond_down_project': _L0_cond_in['down_project'], 'L0_cond_down_gamma': _L0_cond_in['down_gamma'], 'L0_cond_down_beta': _L0_cond_in['down_beta'], 'L0_cond_up_project': _L0_cond_in['up_project'], 'L0_cond_up_gamma': _L0_cond_in['up_gamma'], 'L0_cond_up_beta': _L0_cond_in['up_beta']}

def reference(x, cond_512, L0_cond_down_project, L0_cond_down_gamma, L0_cond_down_beta, L0_cond_up_project, L0_cond_up_gamma, L0_cond_up_beta):
    import jax
    import jax.numpy as jnp

    def _L0_cond_ref(hidden_states, conditions, down_project, down_gamma, down_beta, up_project, up_gamma, up_beta):
        import jax, jax.numpy as jnp
        import numpy as np
        B, S, D, H, C = (8, 1024, 256, 64, 128)
        INIT_RANGE = 0.01
        dg = conditions @ down_gamma
        db = conditions @ down_beta
        ug = conditions @ up_gamma
        ub = conditions @ up_beta
        w_down = down_project[None, :, :] * dg[:, None, :] + db[:, None, :]
        down = jnp.einsum('bsd,bdh->bsh', hidden_states, w_down)
        act = jax.nn.relu(down)
        w_up = up_project[None, :, :] * ug[:, None, :] + ub[:, None, :]
        up = jnp.einsum('bsh,bhd->bsd', act, w_up)
        return up + hidden_states
    x = x + _L0_cond_ref(x, cond_512, L0_cond_down_project, L0_cond_down_gamma, L0_cond_down_beta, L0_cond_up_project, L0_cond_up_gamma, L0_cond_up_beta)
    return x

_drawn_inputs = setup_inputs


def setup_inputs(seed=0):
    import zlib

    import numpy as np

    out = dict(_drawn_inputs(seed))
    spreads = {'L0_cond_down_beta': (0.0, 0.1), 'L0_cond_up_beta': (0.0, 0.1)}
    factors = {'L0_cond_down_project': 2.7, 'L0_cond_down_gamma': 2.726, 'L0_cond_up_gamma': 2.7}
    for name, (base, spread) in spreads.items():
        noise = np.random.default_rng([zlib.crc32(name.encode()), seed]).standard_normal(out[name].shape)
        drawn = base * np.exp(spread * noise) if base else spread * noise
        out[name] = jnp.asarray(drawn.astype(out[name].dtype))
    for name, factor in factors.items():
        out[name] = (out[name] * factor).astype(out[name].dtype)
    return out
```

```python
from contextlib import ExitStack

import concourse.bass as bass
from concourse import mybir

F32 = mybir.dt.float32
BF16 = mybir.dt.bfloat16
ALU = mybir.AluOpType
ACT = mybir.ActivationFunctionType

P = 128
B, S, D = 64, 64, 256
H, C = 64, 128
J = P // S
NQ = B // J
T = 4
NG = NQ // T
DC = D // P
NT = T * S
PARTS = 3
BH = B // 2
QH = NQ // 2


def adapter_kernel(nc, x, cond, down_project, down_gamma, down_beta,
                   up_project, up_gamma, up_beta, out):
    x_groups = x.rearrange("(g i j) s d -> g (j s) i d", i=T, j=J)
    out_groups = out.rearrange("(g i j) s d -> g (j s) i d", i=T, j=J)

    with ExitStack() as ctx:
        def sbuf(name, shape, dt=F32):
            return ctx.enter_context(nc.sbuf_tensor(name, shape, dt))

        def bank(name, dt=F32):
            return ctx.enter_context(nc.psum_tensor(name, [P, 512], dt))

        def sem(name):
            return ctx.enter_context(nc.semaphore(name))

        x_sb = sbuf("x_sb", [P, NG, T, D])
        out_sb = sbuf("out_sb", [P, NG, T, D])
        cond_sb = sbuf("cond_sb", [B, C])
        up_cond = sbuf("up_cond", [C, 2, D])
        down_cond = sbuf("down_cond", [C, 2, J, H])
        dp_sb = sbuf("dp_sb", [P, DC, H])
        up_sb = sbuf("up_sb", [P, 2, D])
        ident = sbuf("ident", [P, P])
        ones = sbuf("ones", [P, H])
        onehot = sbuf("onehot", [PARTS * BH, BH], BF16)
        spread = sbuf("spread", [PARTS * BH, BH, H], BF16)
        condT = sbuf("condT", [C, B])
        condT3 = sbuf("condT3", [C, 2, PARTS, BH])
        parts = sbuf("parts", [PARTS * BH, 2, 2 * D], BF16)
        rest = sbuf("rest", [PARTS * BH, 2, 2 * D])
        coef = sbuf("coef", [P, NG, 2, T])
        xT = sbuf("xT", [P, 2, DC, T, J, S])
        scaled = sbuf("scaled", [P, 2, 2, T, S])
        down_sum = sbuf("down_sum", [P, 2, T, S])
        act = sbuf("act", [P, 2, T, P])
        w_mul = sbuf("w_mul", [P, NQ, D])
        w_add = sbuf("w_add", [P, NQ, D])
        w_up = sbuf("w_up", [P, NQ, D])

        xT_ps = [bank(f"xT_ps{c}") for c in range(DC)]
        down_ps = [bank(f"down_ps{n}") for n in range(2)]
        up_ps = [bank(f"up_ps{n}") for n in range(T // 2)]
        ug_ps = bank("ug_ps")
        ub_ps = bank("ub_ps")

        x_in = [sem(f"x_in{g}") for g in range(NG)]
        cond_in = sem("cond_in")
        up_cond_in = sem("up_cond_in")
        down_cond_in = sem("down_cond_in")
        dp_in = sem("dp_in")
        up_in = sem("up_in")
        out_done = sem("out_done")
        zeroed = sem("zeroed")
        consts_ready = sem("consts_ready")
        spread_ready = sem("spread_ready")
        condT_ps_ready = sem("condT_ps_ready")
        condT_ready = sem("condT_ready")
        coef_ps_ready = sem("coef_ps_ready")
        coef_ready = sem("coef_ready")
        rows_ps_ready = sem("rows_ps_ready")
        high_ready = sem("high_ready")
        rest_ready = sem("rest_ready")
        middle_ready = sem("middle_ready")
        rest2_ready = sem("rest2_ready")
        parts_ready = sem("parts_ready")
        xT_ps_ready = sem("xT_ps_ready")
        xT_ready = sem("xT_ready")
        ugb_ps_ready = sem("ugb_ps_ready")
        w_mul_ready = sem("w_mul_ready")
        w_add_ready = sem("w_add_ready")
        w_up_ready = sem("w_up_ready")
        down_ps_ready = sem("down_ps_ready")
        scaled_ready = sem("scaled_ready")
        down_ready = sem("down_ready")
        act_ready = sem("act_ready")
        up_ps_ready = sem("up_ps_ready")
        out_ready = sem("out_ready")

        block = ctx.enter_context(nc.Block())

        @block.sync
        def _(sp):
            sp.dma_start(x_sb[:, 0], x_groups[0]).then_inc(x_in[0], 16)
            sp.dma_start(dp_sb[:, :, :], down_project.rearrange("(c p) h -> p c h", p=P)).then_inc(dp_in, 16)
            for g in range(1, NG):
                sp.dma_start(x_sb[:, g], x_groups[g]).then_inc(x_in[g], 16)
            for g in range(NG):
                sp.wait_ge(out_ready, 2 * (g + 1))
                sp.dma_start(out_groups[g], out_sb[:, g]).then_inc(out_done, 16)
            sp.wait_ge(out_done, 16 * NG)

        @block.gpsimd
        def _(pool):
            nc.gpsimd.memset(ident[:, :], 0.0).then_inc(zeroed, 1)
            nc.gpsimd.memset(onehot[:, :], 0.0).then_inc(zeroed, 1)
            pool.wait_ge(zeroed, 1)
            nc.gpsimd.affine_select(out=ident[:, :], in_=ident[:, :], compare_op=ALU.not_equal, fill=1.0,
                                    base=0, pattern=[[-1, P]], channel_multiplier=1).then_inc(consts_ready, 1)
            for part in range(PARTS):
                pool.wait_ge(zeroed, 2 + part)
                select = nc.gpsimd.affine_select(out=onehot[:, :], in_=onehot[:, :], compare_op=ALU.not_equal,
                                                 fill=1.0, base=-BH * part, pattern=[[-1, BH]],
                                                 channel_multiplier=1)
                select.then_inc(zeroed if part < PARTS - 1 else consts_ready, 1)
            pool.wait_ge(consts_ready, 2)
            for k in range(4):
                cols = slice(k * BH // 4, (k + 1) * BH // 4)
                nc.gpsimd.tensor_copy(spread[:, cols, :], onehot[:, cols].unsqueeze(2).to_broadcast(
                    [PARTS * BH, BH // 4, H])).then_inc(spread_ready, 1)
                if k == 0:
                    nc.gpsimd.memset(ones[:, :], 1.0).then_inc(consts_ready, 1)
            nc.gpsimd.memset(act[:, :, :, :], 0.0).then_inc(consts_ready, 1)
            for n in range(NQ // 2):
                pool.wait_ge(w_mul_ready, n + 1)
                pool.wait_ge(w_add_ready, n + 1)
                nc.gpsimd.tensor_tensor(w_up[:, 2 * n:2 * n + 2, :], w_mul[:, 2 * n:2 * n + 2, :],
                                        w_add[:, 2 * n:2 * n + 2, :], ALU.add).then_inc(w_up_ready, 1)

        @block.scalar
        def _(act_e):
            act_e.dma_start(cond_sb[:, :], cond).then_inc(cond_in, 16)
            for k, src in enumerate((up_gamma, up_beta)):
                act_e.dma_start(up_cond[:, k, :], src).then_inc(up_cond_in, 16)
            for k, src in enumerate((down_gamma, down_beta)):
                for j in range(J):
                    act_e.dma_start(down_cond[:, k, j, :], src).then_inc(down_cond_in, 16)
            for k in range(2):
                for j in range(J):
                    act_e.dma_start(up_sb[j * H:(j + 1) * H, k, :], up_project).then_inc(up_in, 16)

            for n, rows in enumerate((ug_ps, ub_ps)):
                act_e.wait_ge(rows_ps_ready, n + 1)
                nc.scalar.activation(parts[:, n, :], rows[0:PARTS * BH, :], ACT.Copy).then_inc(high_ready, 1)

            def move_xT(g):
                for c in range(DC):
                    act_e.wait_ge(xT_ps_ready, DC * g + c + 1)
                    if c == 0 and g >= 2:
                        act_e.wait_ge(down_ps_ready, g - 1)
                    nc.scalar.activation(xT[:, g % 2, c].rearrange("p i j s -> p (i j s)"), xT_ps[c][:, :],
                                         ACT.Copy).then_inc(xT_ready, 1)

            def move_ub(n):
                act_e.wait_ge(ugb_ps_ready, n + 1)
                nc.scalar.activation(w_add[:, 2 * n:2 * n + 2, :].rearrange("p q d -> p (q d)"), ub_ps[:, :],
                                     ACT.Copy).then_inc(w_add_ready, 1)

            def relu(g):
                act_e.wait_ge(down_ready, g + 1)
                if g == 0:
                    act_e.wait_ge(consts_ready, 4)
                if g >= 2:
                    act_e.wait_ge(up_ps_ready, 2 * (g - 1))
                for j in range(J):
                    rows = slice(j * H, (j + 1) * H)
                    nc.scalar.activation(act[rows, g % 2, :, j * S:(j + 1) * S], down_sum[rows, g % 2],
                                         ACT.Relu).then_inc(act_ready, 1)

            for step in range(NG + 1):
                if step < NG:
                    move_xT(step)
                    move_ub(2 * step)
                if step >= 1:
                    relu(step - 1)
                if step < NG:
                    move_ub(2 * step + 1)

        @block.vector
        def _(dve):
            dve.wait_ge(condT_ps_ready, 1)
            nc.vector.tensor_copy(condT[:, :], xT_ps[0][:, 0:B]).then_inc(condT_ready, 1)
            dve.wait_ge(condT_ready, 1)
            halves = condT[:, :].rearrange("p (n b) -> p n b", b=BH)
            for part in range(PARTS):
                nc.vector.tensor_copy(condT3[:, :, part, :], halves).then_inc(condT_ready, 1)
            dve.wait_ge(coef_ps_ready, 1)
            for k in range(2):
                for j in range(J):
                    rows = slice(j * H, (j + 1) * H)
                    src = xT_ps[1][rows, k * B:(k + 1) * B].rearrange("p (g i j) -> p g i j", i=T, j=J)
                    nc.vector.tensor_copy(coef[rows, :, k, :], src[:, :, :, j]).then_inc(coef_ready, 1)
            mid, low = slice(BH, 2 * BH), slice(2 * BH, 3 * BH)
            for n, rows in enumerate((ug_ps, ub_ps)):
                dve.wait_ge(high_ready, n + 1)
                nc.vector.tensor_tensor(rest[:, n, :], rows[0:PARTS * BH, :], parts[:, n, :],
                                        ALU.subtract).then_inc(rest_ready, 1)
                dve.wait_ge(rest_ready, n + 1)
                nc.vector.tensor_copy(parts[low, n, :], rest[low, n, :]).then_inc(middle_ready, 1)
                nc.vector.tensor_copy(parts[mid, n, :], rest[mid, n, :]).then_inc(parts_ready, 1)
                dve.wait_ge(middle_ready, n + 1)
                nc.vector.tensor_tensor(rest[low, n, :], rest[low, n, :], parts[low, n, :],
                                        ALU.subtract).then_inc(rest2_ready, 1)
                dve.wait_ge(rest2_ready, n + 1)
                nc.vector.tensor_copy(parts[low, n, :], rest[low, n, :]).then_inc(parts_ready, 1)

            def multiply_w(n):
                dve.wait_ge(ugb_ps_ready, n + 1)
                if n == 0:
                    dve.wait_ge(up_in, 16 * 2 * J)
                nc.vector.tensor_tensor(w_mul[:, 2 * n:2 * n + 2, :].rearrange("p q d -> p (q d)"), ug_ps[:, :],
                                        up_sb[:, :, :].rearrange("p k d -> p (k d)"), ALU.mult).then_inc(w_mul_ready, 1)

            def add_x(g):
                for n in range(T // 2):
                    dve.wait_ge(up_ps_ready, 2 * g + n + 1)
                    tiles = slice(2 * n, 2 * n + 2)
                    nc.vector.scalar_tensor_tensor(
                        out=out_sb[:, g, tiles, :].rearrange("p i d -> p (i d)"),
                        in0=x_sb[:, g, tiles, :].rearrange("p i d -> p (i d)"), scalar=2.0,
                        in1=up_ps[n][:, :], op0=ALU.mult, op1=ALU.add).then_inc(out_ready, 1)

            def scale_down(g):
                dve.wait_ge(down_ps_ready, g + 1)
                if g >= 2:
                    dve.wait_ge(act_ready, J * (g - 1))
                factors = coef[:, g].rearrange("p k i -> p (k i)").unsqueeze(2).to_broadcast([P, 2 * T, S])
                nc.vector.tensor_tensor(scaled[:, g % 2].rearrange("p k i s -> p (k i) s"),
                                        down_ps[g % 2][:, :].rearrange("p (n s) -> p n s", s=S),
                                        factors, ALU.mult).then_inc(scaled_ready, 1)
                dve.wait_ge(scaled_ready, g + 1)
                nc.vector.tensor_tensor(down_sum[:, g % 2], scaled[:, g % 2, 0], scaled[:, g % 2, 1],
                                        ALU.add).then_inc(down_ready, 1)

            for step in range(NG + 2):
                if step < NG:
                    multiply_w(2 * step)
                if step >= 2:
                    add_x(step - 2)
                if step < NG:
                    multiply_w(2 * step + 1)
                    if step == 0:
                        dve.wait_ge(coef_ready, 2 * J)
                    scale_down(step)

        @block.tensor
        def _(pe):
            mm = nc.tensor.matmul
            pe.wait_ge(consts_ready, 1)
            pe.wait_ge(cond_in, 16)
            nc.tensor.transpose(xT_ps[0][:, 0:B], cond_sb[:, :], ident[0:B, 0:B]).then_inc(condT_ps_ready, 1)
            pe.wait_ge(condT_ready, 1)
            pe.wait_ge(down_cond_in, 16 * 2 * J)
            for k in range(2):
                last = mm(xT_ps[1][:, k * B:(k + 1) * B], down_cond[:, k].rearrange("p j h -> p (j h)"),
                          condT[:, :], start=True, stop=True)
            last.then_inc(coef_ps_ready, 1)
            pe.wait_ge(condT_ready, 1 + PARTS)
            pe.wait_ge(up_cond_in, 32)
            for n, rows in enumerate((ug_ps, ub_ps)):
                mm(rows[0:PARTS * BH, :], condT3[:, n].rearrange("p k b -> p (k b)"),
                   up_cond[:, :, :].rearrange("p k d -> p (k d)"), start=True, stop=True).then_inc(rows_ps_ready, 1)

            def transpose_x(g):
                pe.wait_ge(x_in[g], 16)
                for c in range(DC):
                    if g >= 1:
                        pe.wait_ge(xT_ready, DC * (g - 1) + c + 1)
                    elif c == 1:
                        pe.wait_ge(coef_ready, 2 * J)
                    for i in range(T):
                        last = nc.tensor.transpose(xT_ps[c][:, i * P:(i + 1) * P],
                                                   x_sb[:, g, i, c * P:(c + 1) * P], ident[:, :])
                    last.then_inc(xT_ps_ready, 1)

            def spread_rows(n):
                if n == 0:
                    pe.wait_ge(parts_ready, 4)
                else:
                    pe.wait_ge(w_mul_ready, n)
                    pe.wait_ge(w_add_ready, n)
                if 2 * n < QH:
                    pe.wait_ge(spread_ready, 2 * J * n * 4 // BH + 1)
                for q in (2 * n, 2 * n + 1):
                    first = J * (q % QH)
                    pick = spread[:, first:first + J, :].rearrange("p b h -> p (b h)")
                    for k, rows in enumerate((ug_ps, ub_ps)):
                        last = mm(rows[:, (q % 2) * D:(q % 2 + 1) * D], pick,
                                  parts[:, q // QH, k * D:(k + 1) * D], start=True, stop=True)
                last.then_inc(ugb_ps_ready, 1)

            def down(g):
                pe.wait_ge(xT_ready, DC * (g + 1))
                if g == 0:
                    pe.wait_ge(dp_in, 16)
                    pe.wait_ge(consts_ready, 3)
                if g >= 2:
                    pe.wait_ge(scaled_ready, g - 1)
                for cols, weights in ((slice(0, NT), [dp_sb[:, c, :] for c in range(DC)]),
                                      (slice(NT, 2 * NT), [ones[:, :]] * DC)):
                    for c in range(DC):
                        for j in range(J):
                            last = mm(down_ps[g % 2][j * H:(j + 1) * H, cols], weights[c],
                                      xT[:, g % 2, c, :, j, :], start=c == 0, stop=c == DC - 1)
                last.then_inc(down_ps_ready, 1)

            def up(g):
                pe.wait_ge(act_ready, J * (g + 1))
                for n in range(T // 2):
                    pe.wait_ge(w_up_ready, 2 * g + n + 1)
                    if g >= 1:
                        pe.wait_ge(out_ready, 2 * (g - 1) + n + 1)
                    for i in (2 * n, 2 * n + 1):
                        last = mm(up_ps[n][:, (i % 2) * D:(i % 2 + 1) * D], act[:, g % 2, i, :],
                                  w_up[:, T * g + i, :], start=True, stop=True)
                    last.then_inc(up_ps_ready, 1)

            for step in range(NG + 2):
                if step < NG:
                    transpose_x(step)
                    spread_rows(2 * step)
                if step >= 2:
                    up(step - 2)
                if step < NG:
                    spread_rows(2 * step + 1)
                    down(step)


_INS = ['x', 'cond_512', 'L0_cond_down_project', 'L0_cond_down_gamma', 'L0_cond_down_beta',
        'L0_cond_up_project', 'L0_cond_up_gamma', 'L0_cond_up_beta']


def kernel(**inputs):
    import numpy as _np
    import concourse.bacc as _bacc
    from concourse import mybir as _mybir
    from concourse.bass_utils import run_bass_kernel_spmd as _run

    nc = _bacc.Bacc("TRN2", target_bir_lowering=False, num_devices=1)
    arrays, args = {}, []
    for name in _INS:
        a = _np.ascontiguousarray(inputs[name])
        arrays[f"in_{name}"] = a
        args.append(nc.dram_tensor(f"in_{name}", a.shape, _mybir.dt.from_np(a.dtype), kind="ExternalInput").ap())
    args.append(nc.dram_tensor("out_0", (B, S, D), F32, kind="ExternalOutput").ap())
    adapter_kernel(nc, *args)
    r = _run(nc, [arrays], core_ids=[0])
    return r.results[0]["out_0"]
```

```python
from contextlib import ExitStack

import concourse.bass as bass
from concourse import mybir

F32 = mybir.dt.float32
BF16 = mybir.dt.bfloat16
ALU = mybir.AluOpType
ACT = mybir.ActivationFunctionType

P = 128
B, S, D = 64, 64, 256
H, C = 64, 128
J = P // S
NQ = B // J
T = 4
NG = NQ // T
DC = D // P
NT = T * S
PARTS = 3
BH = B // 2
QH = NQ // 2
ACT_SLOTS = 4
W_SLOTS = 4
DVE_SUMS = 2
WARM = 4


def adapter_kernel(nc, x, cond, down_project, down_gamma, down_beta,
                   up_project, up_gamma, up_beta, out):
    x_groups = x.rearrange("(g i j) s d -> g (j s) i d", i=T, j=J)
    out_groups = out.rearrange("(g i j) s d -> g (j s) i d", i=T, j=J)

    with ExitStack() as ctx:
        def sbuf(name, shape, dt=F32):
            return ctx.enter_context(nc.sbuf_tensor(name, shape, dt))

        def bank(name, dt=F32):
            return ctx.enter_context(nc.psum_tensor(name, [P, 512], dt))

        def sem(name):
            return ctx.enter_context(nc.semaphore(name))

        x_sb = sbuf("x_sb", [P, NG, T, D])
        out_sb = sbuf("out_sb", [P, NG, T, D])
        cond_sb = sbuf("cond_sb", [B, C])
        up_cond = sbuf("up_cond", [C, 2, D])
        down_cond = sbuf("down_cond", [C, 2, J, H])
        dp_sb = sbuf("dp_sb", [P, DC, H])
        up_sb = sbuf("up_sb", [P, 2, D])
        ident = sbuf("ident", [P, P])
        fold = sbuf("fold", [P, S])
        same_half = sbuf("same_half", [P, J, H])
        onehot = sbuf("onehot", [PARTS * BH, BH], BF16)
        spread = sbuf("spread", [PARTS * BH, BH, H], BF16)
        condT = sbuf("condT", [C, B])
        condT3 = sbuf("condT3", [C, 2, PARTS, BH])
        parts = sbuf("parts", [PARTS * BH, 2, 2 * D], BF16)
        rest = sbuf("rest", [PARTS * BH, 2, 2 * D])
        coef = sbuf("coef", [P, NG, 2, T])
        xT = sbuf("xT", [P, 2, DC, T, J, S])
        row_sum = sbuf("row_sum", [P, NG, T])
        sum_diag = sbuf("sum_diag", [P, 2, T, S])
        scaled = sbuf("scaled", [P, 2, 2, T, S])
        down_sum = sbuf("down_sum", [P, 2, T, S])
        act = sbuf("act", [P, ACT_SLOTS, T, P])
        w_mul = sbuf("w_mul", [P, W_SLOTS, 2 * D])
        w_add = sbuf("w_add", [P, W_SLOTS, 2 * D])
        w_up = sbuf("w_up", [P, NQ, D])

        xT_ps = [bank(f"xT_ps{c}") for c in range(DC)]
        down_ps = [bank(f"down_ps{n}") for n in range(2)]
        up_ps = [bank(f"up_ps{n}") for n in range(T // 2)]
        ug_ps = bank("ug_ps")
        ub_ps = bank("ub_ps")

        x_in = [sem(f"x_in{g}") for g in range(NG)]
        cond_in = sem("cond_in")
        up_cond_in = sem("up_cond_in")
        down_cond_in = sem("down_cond_in")
        dp_in = sem("dp_in")
        up_in = sem("up_in")
        out_done = sem("out_done")
        zeroed = sem("zeroed")
        ident_ready = sem("ident_ready")
        onehot_ready = sem("onehot_ready")
        fold_ready = sem("fold_ready")
        same_half_ready = sem("same_half_ready")
        spread_ready = sem("spread_ready")
        act_zeroed = sem("act_zeroed")
        condT_ps_ready = sem("condT_ps_ready")
        condT_ready = sem("condT_ready")
        coef_ps_ready = sem("coef_ps_ready")
        coef_ready = sem("coef_ready")
        rows_ps_ready = sem("rows_ps_ready")
        high_ready = sem("high_ready")
        rest_ready = sem("rest_ready")
        middle_ready = sem("middle_ready")
        rest2_ready = sem("rest2_ready")
        parts_ready = sem("parts_ready")
        xT_ps_ready = sem("xT_ps_ready")
        xT_ready = sem("xT_ready")
        dve_sums_ready = sem("dve_sums_ready")
        act_sums_ready = sem("act_sums_ready")
        sum_diag_ready = sem("sum_diag_ready")
        ugb_ps_ready = sem("ugb_ps_ready")
        w_mul_ready = sem("w_mul_ready")
        w_add_ready = sem("w_add_ready")
        w_up_ready = sem("w_up_ready")
        down_ps_ready = sem("down_ps_ready")
        scaled_ready = sem("scaled_ready")
        down_ready = sem("down_ready")
        act_ready = sem("act_ready")
        up_ps_ready = sem("up_ps_ready")
        out_ready = sem("out_ready")

        block = ctx.enter_context(nc.Block())

        STEPS = range(-2, NG + 1)

        @block.sync
        def _(sp):
            sp.dma_start(cond_sb[:, :], cond).then_inc(cond_in, 16)
            sp.dma_start(up_cond[:, 0, :], up_gamma).then_inc(up_cond_in, 16)
            sp.dma_start(x_sb[:, 0], x_groups[0]).then_inc(x_in[0], 16)
            sp.dma_start(dp_sb[:, :, :], down_project.rearrange("(c p) h -> p c h", p=P)).then_inc(dp_in, 16)
            for g in range(1, NG):
                sp.dma_start(x_sb[:, g], x_groups[g]).then_inc(x_in[g], 16)
                if g == 1:
                    for j in range(J):
                        sp.dma_start(up_sb[j * H:(j + 1) * H, :, :],
                                     up_project.unsqueeze(1).to_broadcast([H, 2, D])).then_inc(up_in, 16)
            for g in range(NG - 1):
                sp.wait_ge(out_ready, 2 * (g + 1))
                sp.dma_start(out_groups[g], out_sb[:, g]).then_inc(out_done, 16)
            for n in range(T // 2):
                sp.wait_ge(out_ready, 2 * (NG - 1) + n + 1)
                tiles = slice(2 * n, 2 * n + 2)
                sp.dma_start(out_groups[NG - 1][:, tiles, :], out_sb[:, NG - 1, tiles, :]).then_inc(out_done, 16)
            sp.wait_ge(out_done, 16 * (NG + 1))

        @block.gpsimd
        def _(pool):
            nc.gpsimd.memset(ident[:, :], 0.0).then_inc(zeroed, 1)
            pool.wait_ge(zeroed, 1)
            nc.gpsimd.affine_select(out=ident[:, :], in_=ident[:, :], compare_op=ALU.not_equal, fill=1.0,
                                    base=0, pattern=[[-1, P]], channel_multiplier=1).then_inc(ident_ready, 1)
            nc.gpsimd.memset(onehot[:, :], 0.0).then_inc(zeroed, 1)
            nc.gpsimd.memset(fold[:, :], 0.0).then_inc(zeroed, 1)
            pool.wait_ge(zeroed, 3)
            for part in range(PARTS):
                if part >= 1:
                    pool.wait_ge(onehot_ready, part)
                nc.gpsimd.affine_select(out=onehot[:, :], in_=onehot[:, :], compare_op=ALU.not_equal,
                                        fill=1.0, base=-BH * part, pattern=[[-1, BH]],
                                        channel_multiplier=1).then_inc(onehot_ready, 1)
            for j in range(J):
                if j >= 1:
                    pool.wait_ge(fold_ready, j)
                nc.gpsimd.affine_select(out=fold[:, :], in_=fold[:, :], compare_op=ALU.not_equal,
                                        fill=1.0, base=-S * j, pattern=[[-1, S]],
                                        channel_multiplier=1).then_inc(fold_ready, 1)

            def widen(k):
                if k == 0:
                    pool.wait_ge(onehot_ready, PARTS)
                cols = slice(k * BH // 4, (k + 1) * BH // 4)
                nc.gpsimd.tensor_copy(spread[:, cols, :], onehot[:, cols].unsqueeze(2).to_broadcast(
                    [PARTS * BH, BH // 4, H])).then_inc(spread_ready, 1)

            def place_sums(g):
                pool.wait_ge(dve_sums_ready, g + 1)
                pool.wait_ge(act_sums_ready, (T - DVE_SUMS) * (g + 1))
                if g == 0:
                    pool.wait_ge(fold_ready, J)
                if g >= 2:
                    pool.wait_ge(down_ps_ready, g - 1)
                nc.gpsimd.tensor_tensor(sum_diag[:, g % 2], fold[:, :].unsqueeze(1).to_broadcast([P, T, S]),
                                        row_sum[:, g, :].unsqueeze(2).to_broadcast([P, T, S]),
                                        ALU.mult).then_inc(sum_diag_ready, 1)

            def add_w(n):
                pool.wait_ge(w_mul_ready, n + 1)
                pool.wait_ge(w_add_ready, n + 1)
                nc.gpsimd.tensor_tensor(w_up[:, 2 * n:2 * n + 2, :].rearrange("p q d -> p (q d)"),
                                        w_mul[:, n % W_SLOTS, :], w_add[:, n % W_SLOTS, :],
                                        ALU.add).then_inc(w_up_ready, 1)

            for s in STEPS:
                if s < 2:
                    widen(s + 2)
                if s + 2 < NG:
                    place_sums(s + 2)
                if 0 <= s + 1 < NG:
                    add_w(2 * (s + 1))
                    add_w(2 * (s + 1) + 1)

        @block.scalar
        def _(act_e):
            act_e.dma_start(up_cond[:, 1, :], up_beta).then_inc(up_cond_in, 16)
            for k, src in enumerate((down_gamma, down_beta)):
                act_e.dma_start(down_cond[:, k], src.unsqueeze(1).to_broadcast([C, J, H])).then_inc(down_cond_in, 16)

            def high_parts(n, rows):
                act_e.wait_ge(rows_ps_ready, n + 1)
                nc.scalar.activation(parts[:, n, :], rows[0:PARTS * BH, :], ACT.Copy).then_inc(high_ready, 1)

            def move_xT(g):
                for c in range(DC):
                    act_e.wait_ge(xT_ps_ready, DC * g + c + 1)
                    if c == 0 and g >= 2:
                        act_e.wait_ge(down_ps_ready, g - 1)
                    nc.scalar.activation(xT[:, g % 2, c].rearrange("p i j s -> p (i j s)"), xT_ps[c][:, :],
                                         ACT.Copy).then_inc(xT_ready, 1)

            def row_sums(g):
                act_e.wait_ge(x_in[g], 16)
                for i in range(DVE_SUMS, T):
                    nc.scalar.activation(out_sb[:, g, i, :], x_sb[:, g, i, :], ACT.Copy,
                                         accum_out=row_sum[:, g, i:i + 1]).then_inc(act_sums_ready, 1)

            def move_ub(n):
                act_e.wait_ge(ugb_ps_ready, n + 1)
                if n >= W_SLOTS:
                    act_e.wait_ge(w_up_ready, n - W_SLOTS + 1)
                nc.scalar.activation(w_add[:, n % W_SLOTS, :], ub_ps[:, :], ACT.Copy).then_inc(w_add_ready, 1)

            def relu(g):
                act_e.wait_ge(down_ready, g + 1)
                if g == 0:
                    act_e.wait_ge(act_zeroed, 1)
                if g >= ACT_SLOTS:
                    act_e.wait_ge(up_ps_ready, 2 * (g - ACT_SLOTS + 1))
                for j in range(J):
                    rows = slice(j * H, (j + 1) * H)
                    nc.scalar.activation(act[rows, g % ACT_SLOTS, :, j * S:(j + 1) * S],
                                         down_sum[rows, g % 2], ACT.Relu).then_inc(act_ready, 1)

            for s in STEPS:
                if s == -2:
                    high_parts(0, ug_ps)
                if s + 2 < NG:
                    move_xT(s + 2)
                if s == 0:
                    high_parts(1, up_ps[0])
                if 0 <= s + 1 < NG:
                    move_ub(2 * (s + 1))
                if 0 <= s < NG:
                    relu(s)
                if s + 2 < NG:
                    row_sums(s + 2)
                if 0 <= s + 1 < NG:
                    move_ub(2 * (s + 1) + 1)

        @block.vector
        def _(dve):
            nc.vector.memset(same_half[:, :, :], 0.0).then_inc(same_half_ready, 1)
            nc.vector.memset(act[:, :, :, :], 0.0).then_inc(act_zeroed, 1)
            dve.wait_ge(same_half_ready, 1)
            for j in range(J):
                nc.vector.memset(same_half[j * S:(j + 1) * S, j, :], 1.0).then_inc(same_half_ready, 1)
            dve.wait_ge(condT_ps_ready, 1)
            nc.vector.tensor_copy(condT[:, :], xT_ps[0][:, 0:B]).then_inc(condT_ready, 1)
            dve.wait_ge(condT_ready, 1)
            for part in range(PARTS):
                nc.vector.tensor_copy(condT3[:, :, part, :],
                                      condT[:, :].rearrange("p (n b) -> p n b", b=BH)).then_inc(condT_ready, 1)

            def move_coef():
                dve.wait_ge(coef_ps_ready, 1)
                for k in range(2):
                    for j in range(J):
                        rows = slice(j * H, (j + 1) * H)
                        src = down_ps[1][rows, k * B:(k + 1) * B].rearrange("p (g i j) -> p g i j", i=T, j=J)
                        nc.vector.tensor_copy(coef[rows, :, k, :], src[:, :, :, j]).then_inc(coef_ready, 1)

            def lower_parts(n, rows):
                mid, low = slice(BH, 2 * BH), slice(2 * BH, 3 * BH)
                dve.wait_ge(high_ready, n + 1)
                nc.vector.tensor_tensor(rest[:, n, :], rows[0:PARTS * BH, :], parts[:, n, :],
                                        ALU.subtract).then_inc(rest_ready, 1)
                dve.wait_ge(rest_ready, n + 1)
                nc.vector.tensor_copy(parts[low, n, :], rest[low, n, :]).then_inc(middle_ready, 1)
                nc.vector.tensor_copy(parts[mid, n, :], rest[mid, n, :]).then_inc(parts_ready, 1)
                dve.wait_ge(middle_ready, n + 1)
                nc.vector.tensor_tensor(rest[low, n, :], rest[low, n, :], parts[low, n, :],
                                        ALU.subtract).then_inc(rest2_ready, 1)
                dve.wait_ge(rest2_ready, n + 1)
                nc.vector.tensor_copy(parts[low, n, :], rest[low, n, :]).then_inc(parts_ready, 1)

            def row_sums(g):
                dve.wait_ge(x_in[g], 16)
                nc.vector.tensor_reduce(row_sum[:, g, 0:DVE_SUMS], x_sb[:, g, 0:DVE_SUMS, :],
                                        mybir.AxisListType.X, ALU.add).then_inc(dve_sums_ready, 1)

            def multiply_w(n):
                dve.wait_ge(ugb_ps_ready, n + 1)
                if n == 0:
                    dve.wait_ge(up_in, 16 * J)
                if n >= W_SLOTS:
                    dve.wait_ge(w_up_ready, n - W_SLOTS + 1)
                nc.vector.tensor_tensor(w_mul[:, n % W_SLOTS, :], ug_ps[:, :],
                                        up_sb[:, :, :].rearrange("p k d -> p (k d)"), ALU.mult).then_inc(w_mul_ready, 1)

            def add_x(g):
                for n in range(T // 2):
                    dve.wait_ge(up_ps_ready, 2 * g + n + 1)
                    tiles = slice(2 * n, 2 * n + 2)
                    nc.vector.scalar_tensor_tensor(
                        out=out_sb[:, g, tiles, :].rearrange("p i d -> p (i d)"),
                        in0=x_sb[:, g, tiles, :].rearrange("p i d -> p (i d)"), scalar=2.0,
                        in1=up_ps[n][:, :], op0=ALU.mult, op1=ALU.add).then_inc(out_ready, 1)

            def scale_down(g):
                dve.wait_ge(down_ps_ready, g + 1)
                if g == 0:
                    dve.wait_ge(coef_ready, 2 * J)
                factors = coef[:, g].rearrange("p k i -> p (k i)").unsqueeze(2).to_broadcast([P, 2 * T, S])
                nc.vector.tensor_tensor(scaled[:, g % 2].rearrange("p k i s -> p (k i) s"),
                                        down_ps[g % 2][:, :].rearrange("p (n s) -> p n s", s=S),
                                        factors, ALU.mult).then_inc(scaled_ready, 1)
                dve.wait_ge(scaled_ready, g + 1)
                if g >= 2:
                    dve.wait_ge(act_ready, J * (g - 1))
                nc.vector.tensor_tensor(down_sum[:, g % 2], scaled[:, g % 2, 0], scaled[:, g % 2, 1],
                                        ALU.add).then_inc(down_ready, 1)

            for s in STEPS:
                if s == -2:
                    lower_parts(0, ug_ps)
                    move_coef()
                if 0 <= s + 1 < NG:
                    multiply_w(2 * (s + 1))
                if s + 2 < NG:
                    row_sums(s + 2)
                if s >= 1:
                    add_x(s - 1)
                if s == -1:
                    scale_down(s + 1)
                if 0 <= s + 1 < NG:
                    multiply_w(2 * (s + 1) + 1)
                if 0 < s + 1 < NG:
                    scale_down(s + 1)
                if s == 0:
                    lower_parts(1, up_ps[0])

        @block.tensor
        def _(pe):
            mm = nc.tensor.matmul
            pe.wait_ge(ident_ready, 1)
            for _ in range(WARM):
                mm(down_ps[0][:, 0:P], ident[:, :], ident[:, :], start=True, stop=True)
            pe.wait_ge(cond_in, 16)
            nc.tensor.transpose(xT_ps[0][:, 0:B], cond_sb[:, :], ident[0:B, 0:B]).then_inc(condT_ps_ready, 1)

            def coef_rows():
                pe.wait_ge(condT_ready, 1)
                pe.wait_ge(down_cond_in, 32)
                for k in range(2):
                    last = mm(down_ps[1][:, k * B:(k + 1) * B], down_cond[:, k].rearrange("p j h -> p (j h)"),
                              condT[:, :], start=True, stop=True)
                last.then_inc(coef_ps_ready, 1)

            def batch_rows(n, rows):
                pe.wait_ge(condT_ready, 1 + PARTS)
                pe.wait_ge(up_cond_in, 32)
                mm(rows[0:PARTS * BH, :], condT3[:, n].rearrange("p k b -> p (k b)"),
                   up_cond[:, :, :].rearrange("p k d -> p (k d)"), start=True, stop=True).then_inc(rows_ps_ready, 1)

            def transpose_x(g):
                pe.wait_ge(x_in[g], 16)
                for c in range(DC):
                    if g >= 1:
                        pe.wait_ge(xT_ready, DC * (g - 1) + c + 1)
                    elif c == 0:
                        pe.wait_ge(condT_ready, 1)
                    for i in range(T):
                        last = nc.tensor.transpose(xT_ps[c][:, i * P:(i + 1) * P],
                                                   x_sb[:, g, i, c * P:(c + 1) * P], ident[:, :])
                    last.then_inc(xT_ps_ready, 1)

            def spread_rows(n):
                if n == 0:
                    pe.wait_ge(parts_ready, 2)
                else:
                    pe.wait_ge(w_mul_ready, n)
                    pe.wait_ge(w_add_ready, n)
                if 2 * n == QH:
                    pe.wait_ge(parts_ready, 4)
                if 2 * n < QH:
                    pe.wait_ge(spread_ready, 2 * J * n * 4 // BH + 1)
                for q in (2 * n, 2 * n + 1):
                    first = J * (q % QH)
                    pick = spread[:, first:first + J, :].rearrange("p b h -> p (b h)")
                    for k, rows in enumerate((ug_ps, ub_ps)):
                        last = mm(rows[:, (q % 2) * D:(q % 2 + 1) * D], pick,
                                  parts[:, q // QH, k * D:(k + 1) * D], start=True, stop=True)
                last.then_inc(ugb_ps_ready, 1)

            def down(g):
                pe.wait_ge(xT_ready, DC * (g + 1))
                if g == 0:
                    pe.wait_ge(dp_in, 16)
                    pe.wait_ge(same_half_ready, 1 + J)
                if g == 1:
                    pe.wait_ge(coef_ready, 2 * J)
                if g >= 2:
                    pe.wait_ge(scaled_ready, g - 1)
                for c in range(DC):
                    for j in range(J):
                        mm(down_ps[g % 2][j * H:(j + 1) * H, 0:NT], dp_sb[:, c, :],
                           xT[:, g % 2, c, :, j, :], start=c == 0, stop=c == DC - 1)
                pe.wait_ge(sum_diag_ready, g + 1)
                mm(down_ps[g % 2][:, NT:2 * NT], same_half[:, :, :].rearrange("p j h -> p (j h)"),
                   sum_diag[:, g % 2].rearrange("p i s -> p (i s)"), start=True, stop=True).then_inc(down_ps_ready, 1)

            def up(g, n):
                pe.wait_ge(act_ready, J * (g + 1))
                pe.wait_ge(w_up_ready, 2 * g + n + 1)
                if g >= 1:
                    pe.wait_ge(out_ready, 2 * (g - 1) + n + 1)
                elif n == 0:
                    pe.wait_ge(high_ready, 2)
                    pe.wait_ge(rest_ready, 2)
                for i in (2 * n, 2 * n + 1):
                    last = mm(up_ps[n][:, (i % 2) * D:(i % 2 + 1) * D], act[:, g % ACT_SLOTS, i, :],
                              w_up[:, T * g + i, :], start=True, stop=True)
                last.then_inc(up_ps_ready, 1)

            batch_rows(0, ug_ps)
            for s in STEPS:
                if s + 2 < NG:
                    transpose_x(s + 2)
                if s == -2:
                    coef_rows()
                if s == -1:
                    batch_rows(1, up_ps[0])
                if 0 <= s + 1 < NG:
                    spread_rows(2 * (s + 1))
                if s >= 1:
                    up(s - 1, 0)
                    up(s - 1, 1)
                if s == -1:
                    down(s + 1)
                if 0 <= s + 1 < NG:
                    spread_rows(2 * (s + 1) + 1)
                if 0 < s + 1 < NG:
                    down(s + 1)


_INS = ['x', 'cond_512', 'L0_cond_down_project', 'L0_cond_down_gamma', 'L0_cond_down_beta',
        'L0_cond_up_project', 'L0_cond_up_gamma', 'L0_cond_up_beta']


def kernel(**inputs):
    import numpy as _np
    import concourse.bacc as _bacc
    from concourse import mybir as _mybir
    from concourse.bass_utils import run_bass_kernel_spmd as _run

    nc = _bacc.Bacc("TRN2", target_bir_lowering=False, num_devices=1)
    arrays, args = {}, []
    for name in _INS:
        a = _np.ascontiguousarray(inputs[name])
        arrays[f"in_{name}"] = a
        args.append(nc.dram_tensor(f"in_{name}", a.shape, _mybir.dt.from_np(a.dtype), kind="ExternalInput").ap())
    args.append(nc.dram_tensor("out_0", (B, S, D), F32, kind="ExternalOutput").ap())
    adapter_kernel(nc, *args)
    r = _run(nc, [arrays], core_ids=[0])
    return r.results[0]["out_0"]
```

```python
from contextlib import ExitStack

import concourse.bass as bass
from concourse import mybir

F32 = mybir.dt.float32
BF16 = mybir.dt.bfloat16
ALU = mybir.AluOpType
ACT = mybir.ActivationFunctionType

P = 128
B, S, D = 64, 64, 256
H, C = 64, 128
J = P // S
NQ = B // J
T = 4
NG = NQ // T
DC = D // P
NT = T * S
PARTS = 3
BH = B // 2
QH = NQ // 2
SUM_ROWS = PARTS * T * J
SPLIT_STEPS = 5
ACT_SLOTS = 4
W_SLOTS = 4
DVE_SUMS = 2
LAST_PIECES = (
    (NG - 2, 0, 2, 1), (NG - 2, 2, 2, 2), (NG - 1, 0, 2, 2), (NG - 1, 2, 1, 3), (NG - 1, 3, 1, 4))
WARM = (4, 1)


def adapter_kernel(nc, x, cond, down_project, down_gamma, down_beta,
                   up_project, up_gamma, up_beta, out):
    x_groups = x.rearrange("(g i j) s d -> g (j s) i d", i=T, j=J)
    out_groups = out.rearrange("(g i j) s d -> g (j s) i d", i=T, j=J)

    with ExitStack() as ctx:
        def sbuf(name, shape, dt=F32):
            return ctx.enter_context(nc.sbuf_tensor(name, shape, dt))

        def bank(name, dt=F32):
            return ctx.enter_context(nc.psum_tensor(name, [P, 512], dt))

        def sem(name):
            return ctx.enter_context(nc.semaphore(name))

        x_sb = sbuf("x_sb", [P, NG, T, D])
        out_sb = sbuf("out_sb", [P, NG, T, D])
        cond_sb = sbuf("cond_sb", [B, C])
        up_cond = sbuf("up_cond", [C, 2, D])
        down_cond = sbuf("down_cond", [C, 2, J, H])
        dp_sb = sbuf("dp_sb", [P, DC, H])
        up_sb = sbuf("up_sb", [P, 2, D])
        ident = sbuf("ident", [P, P])
        fold = sbuf("fold", [P, S], BF16)
        half_mask = sbuf("half_mask", [P, J])
        sum_onehot = sbuf("sum_onehot", [SUM_ROWS, T * J], BF16)
        sum_spread = sbuf("sum_spread", [SUM_ROWS, T * J, H], BF16)
        onehot = sbuf("onehot", [PARTS * BH, BH], BF16)
        spread = sbuf("spread", [PARTS * BH, BH, H], BF16)
        condT = sbuf("condT", [C, B])
        condT4 = sbuf("condT4", [C, PARTS + 1, BH])
        parts = sbuf("parts", [P, 2 * D], BF16)
        later_parts = sbuf("later_parts", [PARTS * BH, 2 * D], BF16)
        middle = sbuf("middle", [P, 2 * D], BF16)
        low = sbuf("low", [P, 2 * D], BF16)
        rest = sbuf("rest", [P, 2 * D])
        coef = sbuf("coef", [P, NG, 2, T])
        xT = sbuf("xT", [P, 2, DC, T, J, S])
        row_sum = sbuf("row_sum", [P, NG, T])
        sum_left = sbuf("sum_left", [P, PARTS - 1, T * J])
        sum_parts = sbuf("sum_parts", [P, 2, PARTS, T * J], BF16)
        sumT = sbuf("sumT", [SUM_ROWS, 2, S], BF16)
        scaled = sbuf("scaled", [P, 2, 2, T, S])
        down_sum = sbuf("down_sum", [P, 2, T, S])
        act = sbuf("act", [P, ACT_SLOTS, T, P])
        w_mul = sbuf("w_mul", [P, W_SLOTS, 2 * D])
        w_add = sbuf("w_add", [P, W_SLOTS, 2 * D])
        w_up = sbuf("w_up", [P, NQ, D])

        xT_ps = [bank(f"xT_ps{c}") for c in range(DC)]
        down_ps = [bank(f"down_ps{n}") for n in range(2)]
        up_ps = [bank(f"up_ps{n}") for n in range(T // 2)]
        ug_ps = bank("ug_ps")
        ub_ps = bank("ub_ps")

        x_in = [sem(f"x_in{g}") for g in range(NG)]
        cond_in = sem("cond_in")
        up_cond_in = [sem("up_gamma_in"), sem("up_beta_in")]
        down_cond_in = sem("down_cond_in")
        dp_in = sem("dp_in")
        up_in = sem("up_in")
        out_done = sem("out_done")
        zeroed = sem("zeroed")
        ident_ready = sem("ident_ready")
        onehot_ready = sem("onehot_ready")
        fold_ready = sem("fold_ready")
        half_mask_ready = sem("half_mask_ready")
        sum_onehot_ready = sem("sum_onehot_ready")
        sum_spread_ready = sem("sum_spread_ready")
        spread_ready = sem("spread_ready")
        act_zeroed = sem("act_zeroed")
        condT_ps_ready = sem("condT_ps_ready")
        condT_ready = sem("condT_ready")
        coef_ps_ready = sem("coef_ps_ready")
        coef_ready = sem("coef_ready")
        rows_ps_ready = sem("rows_ps_ready")
        high_ready = sem("high_ready")
        rest_ready = sem("rest_ready")
        middle_ready = sem("middle_ready")
        middle0_ready = sem("middle0_ready")
        low0_ready = sem("low0_ready")
        low_ready = sem("low_ready")
        later_parts_in = sem("later_parts_in")
        xT_ps_ready = sem("xT_ps_ready")
        xT_ready = sem("xT_ready")
        dve_sums_ready = sem("dve_sums_ready")
        act_sums_ready = sem("act_sums_ready")
        sums_split = sem("sums_split")
        sumT_ps_ready = sem("sumT_ps_ready")
        sumT_ready = sem("sumT_ready")
        ugb_ps_ready = sem("ugb_ps_ready")
        w_mul_ready = sem("w_mul_ready")
        w_add_ready = sem("w_add_ready")
        w_up_ready = sem("w_up_ready")
        down_ps_ready = sem("down_ps_ready")
        scaled_ready = sem("scaled_ready")
        down_ready = sem("down_ready")
        act_ready = sem("act_ready")
        up_ps_ready = sem("up_ps_ready")
        out_ready = sem("out_ready")

        block = ctx.enter_context(nc.Block())

        STEPS = range(NG + 1)

        @block.sync
        def _(sp):
            sp.dma_start(cond_sb[:, :], cond).then_inc(cond_in, 16)
            sp.dma_start(up_cond[:, 0, :], up_gamma).then_inc(up_cond_in[0], 16)
            sp.dma_start(x_sb[:, 0], x_groups[0]).then_inc(x_in[0], 16)
            for g in range(1, NG):
                sp.dma_start(x_sb[:, g], x_groups[g]).then_inc(x_in[g], 16)
                if g == 1:
                    sp.dma_start(dp_sb[:, :, :], down_project.rearrange("(c p) h -> p c h", p=P)).then_inc(dp_in, 16)
                    for k, src in enumerate((down_gamma, down_beta)):
                        sp.dma_start(down_cond[:, k], src.unsqueeze(1).to_broadcast([C, J, H])).then_inc(down_cond_in, 16)
                    for j in range(J):
                        sp.dma_start(up_sb[j * H:(j + 1) * H, :, :],
                                     up_project.unsqueeze(1).to_broadcast([H, 2, D])).then_inc(up_in, 16)
            last_block = slice(PARTS * BH, P)
            for part, (src, ready) in enumerate(((parts, high_ready), (middle, middle_ready), (low, low_ready))):
                sp.wait_ge(ready, 1)
                sp.dma_start(later_parts[part * BH:(part + 1) * BH, :], src[last_block, :]).then_inc(later_parts_in, 16)
            for g in range(NG - 2):
                sp.wait_ge(out_ready, 2 * (g + 1))
                sp.dma_start(out_groups[g], out_sb[:, g]).then_inc(out_done, 16)
            for g, first, count, ready in LAST_PIECES:
                sp.wait_ge(out_ready, 2 * g + ready)
                tiles = slice(first, first + count)
                sp.dma_start(out_groups[g][:, tiles, :], out_sb[:, g, tiles, :]).then_inc(out_done, 16)
            sp.wait_ge(out_done, 16 * (NG - 2 + len(LAST_PIECES)))

        @block.gpsimd
        def _(pool):
            nc.gpsimd.memset(ident[:, :], 0.0).then_inc(zeroed, 1)
            pool.wait_ge(zeroed, 1)
            nc.gpsimd.affine_select(out=ident[:, :], in_=ident[:, :], compare_op=ALU.not_equal, fill=1.0,
                                    base=0, pattern=[[-1, P]], channel_multiplier=1).then_inc(ident_ready, 1)
            nc.gpsimd.memset(onehot[:, :], 0.0).then_inc(zeroed, 1)
            nc.gpsimd.memset(fold[:, :], 0.0).then_inc(zeroed, 1)
            pool.wait_ge(zeroed, 3)
            for part in range(PARTS):
                if part >= 1:
                    pool.wait_ge(onehot_ready, part)
                nc.gpsimd.affine_select(out=onehot[:, :], in_=onehot[:, :], compare_op=ALU.not_equal,
                                        fill=1.0, base=-BH * part, pattern=[[-1, BH]],
                                        channel_multiplier=1).then_inc(onehot_ready, 1)
            for j in range(J):
                if j >= 1:
                    pool.wait_ge(fold_ready, j)
                nc.gpsimd.affine_select(out=fold[:, :], in_=fold[:, :], compare_op=ALU.not_equal,
                                        fill=1.0, base=-S * j, pattern=[[-1, S]],
                                        channel_multiplier=1).then_inc(fold_ready, 1)

            nc.gpsimd.memset(sum_onehot[:, :], 0.0).then_inc(sum_onehot_ready, 1)
            for part in range(PARTS):
                pool.wait_ge(sum_onehot_ready, part + 1)
                nc.gpsimd.affine_select(out=sum_onehot[:, :], in_=sum_onehot[:, :], compare_op=ALU.not_equal,
                                        fill=1.0, base=-T * J * part, pattern=[[-1, T * J]],
                                        channel_multiplier=1).then_inc(sum_onehot_ready, 1)
            pool.wait_ge(sum_onehot_ready, 1 + PARTS)
            nc.gpsimd.tensor_copy(sum_spread[:, :, :], sum_onehot[:, :].unsqueeze(2).to_broadcast(
                [SUM_ROWS, T * J, H])).then_inc(sum_spread_ready, 1)

            nc.gpsimd.memset(act[:, :, :, :], 0.0).then_inc(act_zeroed, 1)

            def split_sums(g):
                pool.wait_ge(dve_sums_ready, g + 1)
                pool.wait_ge(act_sums_ready, (T - DVE_SUMS) * (g + 1))
                if g == 0:
                    pool.wait_ge(half_mask_ready, 1 + J)
                if g >= 1:
                    pool.wait_ge(sums_split, SPLIT_STEPS * g)
                if g >= 2:
                    pool.wait_ge(sumT_ps_ready, g - 1)
                high, mid, low_part = [sum_parts[:, g % 2, part] for part in range(PARTS)]
                nc.gpsimd.tensor_tensor(sum_left[:, 0].rearrange("p (i j) -> p i j", j=J),
                                        row_sum[:, g, :].unsqueeze(2).to_broadcast([P, T, J]),
                                        half_mask[:, :].unsqueeze(1).to_broadcast([P, T, J]),
                                        ALU.mult).then_inc(sums_split, 1)
                pool.wait_ge(sums_split, SPLIT_STEPS * g + 1)
                nc.gpsimd.tensor_copy(high, sum_left[:, 0]).then_inc(sums_split, 1)
                pool.wait_ge(sums_split, SPLIT_STEPS * g + 2)
                nc.gpsimd.tensor_tensor(sum_left[:, 1], sum_left[:, 0], high, ALU.subtract).then_inc(sums_split, 1)
                pool.wait_ge(sums_split, SPLIT_STEPS * g + 3)
                nc.gpsimd.tensor_copy(mid, sum_left[:, 1]).then_inc(sums_split, 1)
                pool.wait_ge(sums_split, SPLIT_STEPS * g + 4)
                nc.gpsimd.tensor_tensor(low_part, sum_left[:, 1], mid, ALU.subtract).then_inc(sums_split, 1)

            def add_w(n):
                pool.wait_ge(w_mul_ready, n + 1)
                pool.wait_ge(w_add_ready, n + 1)
                nc.gpsimd.tensor_tensor(w_up[:, 2 * n:2 * n + 2, :].rearrange("p q d -> p (q d)"),
                                        w_mul[:, n % W_SLOTS, :], w_add[:, n % W_SLOTS, :],
                                        ALU.add).then_inc(w_up_ready, 1)

            split_sums(0)
            add_w(0)
            split_sums(1)
            split_sums(2)
            add_w(1)
            for s in STEPS:
                if s >= 1 and s + 2 < NG:
                    split_sums(s + 2)
                if s + 1 < NG:
                    add_w(2 * (s + 1))
                    add_w(2 * (s + 1) + 1)

        @block.scalar
        def _(act_e):
            act_e.dma_start(up_cond[:, 1, :], up_beta).then_inc(up_cond_in[1], 16)
            act_e.wait_ge(rows_ps_ready, 1)
            nc.scalar.activation(parts[:, :], ug_ps[:, :], ACT.Copy).then_inc(high_ready, 1)

            def middle_part():
                rows = slice(BH, 2 * BH)
                act_e.wait_ge(rest_ready, 1)
                nc.scalar.activation(parts[rows, :], rest[rows, :], ACT.Copy).then_inc(middle0_ready, 1)

            def move_xT(g, chunks=range(DC)):
                banks = up_ps if g == 0 else xT_ps
                for c in chunks:
                    act_e.wait_ge(xT_ps_ready, DC * g + c + 1)
                    if c == 0 and g >= 2:
                        act_e.wait_ge(down_ps_ready, g - 1)
                    nc.scalar.activation(xT[:, g % 2, c].rearrange("p i j s -> p (i j s)"), banks[c][:, :],
                                         ACT.Copy).then_inc(xT_ready, 1)

            def row_sums(g, tiles=range(DVE_SUMS, T)):
                act_e.wait_ge(x_in[g], 16)
                for i in tiles:
                    nc.scalar.activation(out_sb[:, g, i, :], x_sb[:, g, i, :], ACT.Copy,
                                         accum_out=row_sum[:, g, i:i + 1]).then_inc(act_sums_ready, 1)

            def move_sumT(g):
                act_e.wait_ge(sumT_ps_ready, g + 1)
                if g >= 2:
                    act_e.wait_ge(down_ps_ready, g - 1)
                nc.scalar.activation(sumT[:, g % 2], down_ps[g % 2][0:SUM_ROWS, NT:NT + S],
                                     ACT.Copy).then_inc(sumT_ready, 1)

            def move_ub(n):
                act_e.wait_ge(ugb_ps_ready, n + 1)
                if n >= W_SLOTS:
                    act_e.wait_ge(w_up_ready, n - W_SLOTS + 1)
                nc.scalar.activation(w_add[:, n % W_SLOTS, :], ub_ps[:, :], ACT.Copy).then_inc(w_add_ready, 1)

            def relu(g):
                act_e.wait_ge(down_ready, g + 1)
                if g == 0:
                    act_e.wait_ge(act_zeroed, 1)
                if g >= ACT_SLOTS:
                    act_e.wait_ge(up_ps_ready, 2 * (g - ACT_SLOTS + 1))
                for j in range(J):
                    rows = slice(j * H, (j + 1) * H)
                    nc.scalar.activation(act[rows, g % ACT_SLOTS, :, j * S:(j + 1) * S],
                                         down_sum[rows, g % 2], ACT.Relu).then_inc(act_ready, 1)

            row_sums(0, [DVE_SUMS])
            move_xT(0, [0])
            middle_part()
            move_xT(0, [1])
            row_sums(0, range(DVE_SUMS + 1, T))
            move_xT(1, [0])
            move_ub(0)
            move_xT(1, [1])
            row_sums(1)
            move_sumT(0)
            move_ub(1)
            for s in STEPS:
                if s == 0:
                    row_sums(2)
                    move_ub(2)
                    move_xT(2, [0])
                    move_sumT(1)
                    move_xT(2, [1])
                elif s + 1 < NG:
                    move_sumT(s + 1)
                    if s + 2 < NG:
                        row_sums(s + 2)
                        move_xT(s + 2)
                    move_ub(2 * (s + 1))
                if s < NG:
                    relu(s)
                if s + 1 < NG:
                    move_ub(2 * (s + 1) + 1)

        @block.vector
        def _(dve):
            nc.vector.memset(half_mask[:, :], 0.0).then_inc(half_mask_ready, 1)
            dve.wait_ge(half_mask_ready, 1)
            for j in range(J):
                nc.vector.memset(half_mask[j * S:(j + 1) * S, j:j + 1], 1.0).then_inc(half_mask_ready, 1)
            dve.wait_ge(condT_ps_ready, 1)
            nc.vector.tensor_copy(condT4[:, 0:PARTS, :], xT_ps[0][:, 0:BH].unsqueeze(1).to_broadcast(
                [C, PARTS, BH])).then_inc(condT_ready, 1)
            nc.vector.tensor_copy(condT4[:, PARTS, :], xT_ps[0][:, BH:B]).then_inc(condT_ready, 1)
            nc.vector.tensor_copy(condT[:, :], xT_ps[0][:, 0:B]).then_inc(condT_ready, 1)

            dve.wait_ge(onehot_ready, PARTS)
            for k in range(2):
                cols = slice(k * BH // 2, (k + 1) * BH // 2)
                nc.vector.tensor_copy(spread[:, cols, :], onehot[:, cols].unsqueeze(2).to_broadcast(
                    [PARTS * BH, BH // 2, H])).then_inc(spread_ready, 1)

            def move_coef():
                dve.wait_ge(coef_ps_ready, 1)
                for k in range(2):
                    for j in range(J):
                        rows = slice(j * H, (j + 1) * H)
                        src = down_ps[1][rows, k * B:(k + 1) * B].rearrange("p (g i j) -> p g i j", i=T, j=J)
                        nc.vector.tensor_copy(coef[rows, :, k, :], src[:, :, :, j]).then_inc(coef_ready, 1)

            def lower_parts():
                block = [slice(k * BH, (k + 1) * BH) for k in range(4)]
                last_two = slice(2 * BH, 4 * BH)
                dve.wait_ge(high_ready, 1)
                nc.vector.tensor_tensor(rest[:, :], ug_ps[:, :], parts[:, :], ALU.subtract).then_inc(rest_ready, 1)
                dve.wait_ge(rest_ready, 1)
                nc.vector.tensor_copy(middle[last_two, :], rest[last_two, :]).then_inc(middle_ready, 1)
                dve.wait_ge(middle_ready, 1)
                for rows, dst, done in ((block[2], parts, low0_ready), (block[3], low, low_ready)):
                    nc.vector.tensor_tensor(dst[rows, :], rest[rows, :], middle[rows, :],
                                            ALU.subtract).then_inc(done, 1)

            def row_sums(g):
                dve.wait_ge(x_in[g], 16)
                nc.vector.tensor_reduce(row_sum[:, g, 0:DVE_SUMS], x_sb[:, g, 0:DVE_SUMS, :],
                                        mybir.AxisListType.X, ALU.add).then_inc(dve_sums_ready, 1)

            def multiply_w(n):
                dve.wait_ge(ugb_ps_ready, n + 1)
                if n == 0:
                    dve.wait_ge(up_in, 16 * J)
                if n >= W_SLOTS:
                    dve.wait_ge(w_up_ready, n - W_SLOTS + 1)
                nc.vector.tensor_tensor(w_mul[:, n % W_SLOTS, :], ug_ps[:, :],
                                        up_sb[:, :, :].rearrange("p k d -> p (k d)"), ALU.mult).then_inc(w_mul_ready, 1)

            def add_x(g):
                count, banks = (2, up_ps) if g < NG - 1 else (1, [ug_ps, ub_ps] + up_ps)
                for n in range(T // count):
                    dve.wait_ge(up_ps_ready, 2 * g + n + 1)
                    tiles = slice(count * n, count * (n + 1))
                    nc.vector.scalar_tensor_tensor(
                        out=out_sb[:, g, tiles, :].rearrange("p i d -> p (i d)"),
                        in0=x_sb[:, g, tiles, :].rearrange("p i d -> p (i d)"), scalar=2.0,
                        in1=banks[n][:, 0:count * D], op0=ALU.mult, op1=ALU.add).then_inc(out_ready, 1)

            def scale_down(g):
                dve.wait_ge(down_ps_ready, g + 1)
                if g == 0:
                    dve.wait_ge(coef_ready, 2 * J)
                factors = coef[:, g].rearrange("p k i -> p (k i)").unsqueeze(2).to_broadcast([P, 2 * T, S])
                nc.vector.tensor_tensor(scaled[:, g % 2].rearrange("p k i s -> p (k i) s"),
                                        down_ps[g % 2][:, :].rearrange("p (n s) -> p n s", s=S),
                                        factors, ALU.mult).then_inc(scaled_ready, 1)
                dve.wait_ge(scaled_ready, g + 1)
                if g >= 2:
                    dve.wait_ge(act_ready, J * (g - 1))
                nc.vector.tensor_tensor(down_sum[:, g % 2], scaled[:, g % 2, 0], scaled[:, g % 2, 1],
                                        ALU.add).then_inc(down_ready, 1)

            row_sums(0)
            lower_parts()
            multiply_w(0)
            move_coef()
            row_sums(1)
            multiply_w(1)
            row_sums(2)
            multiply_w(2)
            scale_down(0)
            for s in STEPS:
                if s >= 1 and s + 2 < NG:
                    row_sums(s + 2)
                if s == NG - 2:
                    multiply_w(2 * (s + 1))
                if s + 1 < NG:
                    scale_down(s + 1)
                if 1 <= s < NG - 2:
                    multiply_w(2 * (s + 1))
                if s >= 1:
                    add_x(s - 1)
                if s + 1 < NG:
                    multiply_w(2 * (s + 1) + 1)

        @block.tensor
        def _(pe):
            mm = nc.tensor.matmul
            pe.wait_ge(ident_ready, 1)
            def keep_warm(n):
                for _ in range(n):
                    mm(down_ps[0][:, 0:P], ident[:, :], ident[:, :], start=True, stop=True)

            keep_warm(WARM[0])
            pe.wait_ge(cond_in, 16)
            nc.tensor.transpose(xT_ps[0][:, 0:B], cond_sb[:, :], ident[0:B, 0:B]).then_inc(condT_ps_ready, 1)
            keep_warm(WARM[1])

            def coef_rows():
                pe.wait_ge(condT_ready, 3)
                pe.wait_ge(down_cond_in, 32)
                for k in range(2):
                    last = mm(down_ps[1][:, k * B:(k + 1) * B], down_cond[:, k].rearrange("p j h -> p (j h)"),
                              condT[:, :], start=True, stop=True)
                last.then_inc(coef_ps_ready, 1)

            def batch_rows():
                pe.wait_ge(condT_ready, 2)
                for k in (1, 0):
                    pe.wait_ge(up_cond_in[k], 16)
                    last = mm(ug_ps[:, k * D:(k + 1) * D], condT4[:, :, :].rearrange("p k b -> p (k b)"),
                              up_cond[:, k, :], start=True, stop=True)
                last.then_inc(rows_ps_ready, 1)

            def transpose_x(g):
                banks = up_ps if g == 0 else xT_ps
                pe.wait_ge(x_in[g], 16)
                for c in range(DC):
                    if g >= 2:
                        pe.wait_ge(xT_ready, DC * (g - 1) + c + 1)
                    elif g == 1 and c == 0:
                        pe.wait_ge(condT_ready, 3)
                    for i in range(T):
                        last = nc.tensor.transpose(banks[c][:, i * P:(i + 1) * P],
                                                   x_sb[:, g, i, c * P:(c + 1) * P], ident[:, :])
                    last.then_inc(xT_ps_ready, 1)

            def spread_rows(n):
                if n == 0:
                    pe.wait_ge(middle0_ready, 1)
                    pe.wait_ge(low0_ready, 1)
                else:
                    pe.wait_ge(w_mul_ready, n)
                    pe.wait_ge(w_add_ready, n)
                if 2 * n == QH:
                    pe.wait_ge(later_parts_in, 16 * PARTS)
                if 2 * n < QH:
                    pe.wait_ge(spread_ready, 2 * J * n * 2 // BH + 1)
                for q in (2 * n, 2 * n + 1):
                    first = J * (q % QH)
                    pick = spread[:, first:first + J, :].rearrange("p b h -> p (b h)")
                    for k, rows in enumerate((ug_ps, ub_ps)):
                        last = mm(rows[:, (q % 2) * D:(q % 2 + 1) * D], pick,
                                  (parts if q < QH else later_parts)[0:PARTS * BH, k * D:(k + 1) * D],
                                  start=True, stop=True)
                last.then_inc(ugb_ps_ready, 1)

            def down(g, chunks=range(DC)):
                if g == 0:
                    pe.wait_ge(dp_in, 16)
                if g == 1:
                    pe.wait_ge(coef_ready, 2 * J)
                if g >= 2:
                    pe.wait_ge(scaled_ready, g - 1)
                for c in chunks:
                    pe.wait_ge(xT_ready, DC * g + c + 1)
                    for j in range(J):
                        mm(down_ps[g % 2][j * H:(j + 1) * H, 0:NT], dp_sb[:, c, :],
                           xT[:, g % 2, c, :, j, :], start=c == 0, stop=c == DC - 1)

            def transpose_sums(g):
                pe.wait_ge(sums_split, SPLIT_STEPS * (g + 1))
                if g == 0:
                    pe.wait_ge(fold_ready, J)
                mm(down_ps[g % 2][0:SUM_ROWS, NT:NT + S], sum_parts[:, g % 2].rearrange("p a b -> p (a b)"),
                   fold[:, :], start=True, stop=True).then_inc(sumT_ps_ready, 1)

            def spread_sums(g):
                pe.wait_ge(sumT_ready, g + 1)
                if g == 0:
                    pe.wait_ge(sum_spread_ready, 1)
                for i in range(T):
                    last = mm(down_ps[g % 2][:, NT + i * S:NT + (i + 1) * S],
                              sum_spread[:, i * J:(i + 1) * J, :].rearrange("p j h -> p (j h)"),
                              sumT[:, g % 2], start=True, stop=True)
                last.then_inc(down_ps_ready, 1)

            def up(g):
                pe.wait_ge(act_ready, J * (g + 1))
                count, banks = (2, up_ps) if g < NG - 1 else (1, [ug_ps, ub_ps] + up_ps)
                for n in range(T // count):
                    pe.wait_ge(w_up_ready, 2 * g + count * n // 2 + 1)
                    if g == 0 and n == 0:
                        pe.wait_ge(xT_ready, DC)
                    if g >= 1 and banks[n] in up_ps:
                        pe.wait_ge(out_ready, 2 * (g - 1) + up_ps.index(banks[n]) + 1)
                    if banks[n] is ug_ps:
                        pe.wait_ge(w_mul_ready, NQ // 2)
                    if banks[n] is ub_ps:
                        pe.wait_ge(w_add_ready, NQ // 2)
                    for i in range(count * n, count * (n + 1)):
                        last = mm(banks[n][:, (i % count) * D:(i % count + 1) * D], act[:, g % ACT_SLOTS, i, :],
                                  w_up[:, T * g + i, :], start=True, stop=True)
                    last.then_inc(up_ps_ready, 1)

            batch_rows()
            transpose_x(0)
            transpose_x(1)
            down(0, [0])
            spread_rows(0)
            coef_rows()
            down(0, [1])
            spread_rows(1)
            transpose_sums(0)
            for s in STEPS:
                if s == 0:
                    down(1)
                    spread_sums(0)
                    spread_rows(2)
                    transpose_x(2)
                    transpose_sums(1)
                    spread_rows(3)
                    spread_sums(1)
                elif s + 1 < NG:
                    down(s + 1)
                    transpose_sums(s + 1)
                    if s + 2 < NG:
                        transpose_x(s + 2)
                        spread_sums(s + 1)
                    spread_rows(2 * (s + 1))
                    if s + 2 == NG:
                        spread_sums(s + 1)
                if s >= 1:
                    up(s - 1)
                if 1 <= s < NG - 1:
                    spread_rows(2 * (s + 1) + 1)


_INS = ['x', 'cond_512', 'L0_cond_down_project', 'L0_cond_down_gamma', 'L0_cond_down_beta',
        'L0_cond_up_project', 'L0_cond_up_gamma', 'L0_cond_up_beta']


def kernel(**inputs):
    import numpy as _np
    import concourse.bacc as _bacc
    from concourse import mybir as _mybir
    from concourse.bass_utils import run_bass_kernel_spmd as _run

    nc = _bacc.Bacc("TRN2", target_bir_lowering=False, num_devices=1)
    arrays, args = {}, []
    for name in _INS:
        a = _np.ascontiguousarray(inputs[name])
        arrays[f"in_{name}"] = a
        args.append(nc.dram_tensor(f"in_{name}", a.shape, _mybir.dt.from_np(a.dtype), kind="ExternalInput").ap())
    args.append(nc.dram_tensor("out_0", (B, S, D), F32, kind="ExternalOutput").ap())
    adapter_kernel(nc, *args)
    r = _run(nc, [arrays], core_ids=[0])
    return r.results[0]["out_0"]
```
